# Optimizing a Trainium2 kernel written in Bass

```python
import numpy as np
import jax
import jax.numpy as jnp

def _softmax(x, axis=-1):
    return jax.nn.softmax(x, axis=axis)

def _gelu(x):
    return jax.nn.gelu(x, approximate=True)

def _silu(x):
    return jax.nn.silu(x)

def _sigmoid(x):
    return jax.nn.sigmoid(x)

def _layernorm(x, axis=-1, eps=1e-05):
    m = jnp.mean(x, axis=axis, keepdims=True)
    v = jnp.var(x, axis=axis, keepdims=True)
    return (x - m) / jnp.sqrt(v + eps)

def _scatter_add(tgt, idx, src, axis=0):
    return tgt.at[idx].add(src)

def _segment_sum(src, seg, n):
    return jax.ops.segment_sum(src, seg, n)
kernel_name = 'mk_cond_resid_d2_seqx_r2_79a8fd'

def setup_inputs(seed: int=0):
    np.random.seed(seed)
    _w = jnp.asarray

    def _rec_inputs():
        import jax
        import jax.numpy as jnp
        _rk = jax.random.key(seed)
        x = -0.000125 + 0.9999 * jax.random.normal(jax.random.fold_in(_rk, 1), (32, 512, 512), jnp.float32)
        _lenS = 512 - jax.random.randint(jax.random.fold_in(_rk, 7), (32,), 0, max(1, 512 // 4) + 1, jnp.int32)
        _lenS2 = 512 - jax.random.randint(jax.random.fold_in(_rk, 8), (32,), 0, max(1, 512 // 4) + 1, jnp.int32)
        cond_1024 = 0.00513981 + 1.0024 * jax.random.normal(jax.random.fold_in(_rk, 11), (32, 512), jnp.float32)
        return (x, cond_1024)
    x, cond_1024 = _rec_inputs()

    def _L0_cond_setup():
        import jax, jax.numpy as jnp
        import numpy as np
        IN_FEATURES = 512
        OUT_FEATURES = 512
        BATCH = 32
        SEQ = 512
        EPS = 1e-08
        key = jax.random.key(seed)
        k1, k2, k3 = jax.random.split(key, 3)
        Efou = jax.random.normal(k1, (BATCH, SEQ, IN_FEATURES), dtype=jnp.float32)
        y = jax.random.normal(k2, (BATCH, IN_FEATURES), dtype=jnp.float32)
        weight = jax.random.normal(k3, (IN_FEATURES, OUT_FEATURES), dtype=jnp.float32)
        return {'Efou': Efou, 'y': y, 'weight': weight}
    _L0_cond_all = _L0_cond_setup()
    _L0_cond_in = {k: v for k, v in _L0_cond_all.items() if k in ('weight',)}
    del _L0_cond_all

    def _L1_cond_setup():
        import jax, jax.numpy as jnp
        import numpy as np
        import math
        N, T, D, H = (128, 256, 512, 512)
        key = jax.random.key(seed)
        k1, k2, k3, k4 = jax.random.split(key, 4)
        x = jax.random.normal(k1, (N, T, D), dtype=jnp.float32)
        h0 = jax.random.normal(k2, (N, H), dtype=jnp.float32)
        Wx = jax.random.normal(k3, (D, H), dtype=jnp.float32) / math.sqrt(D)
        Wh = jax.random.normal(k4, (H, H), dtype=jnp.float32) / math.sqrt(H)
        b = jnp.zeros((H,), dtype=jnp.float32)
        return {'x': x, 'h0': h0, 'Wx': Wx, 'Wh': Wh, 'b': b}
    _L1_cond_all = _L1_cond_setup()
    _L1_cond_in = {k: v for k, v in _L1_cond_all.items() if k in ('Wx', 'Wh', 'b')}
    del _L1_cond_all
    return {'x': x, 'cond_1024': cond_1024, 'L0_cond_weight': _L0_cond_in['weight'], 'L1_cond_Wx': _L1_cond_in['Wx'], 'L1_cond_Wh': _L1_cond_in['Wh'], 'L1_cond_b': _L1_cond_in['b']}

def reference(x, cond_1024, L0_cond_weight, L1_cond_Wx, L1_cond_Wh, L1_cond_b):
    import jax
    import jax.numpy as jnp

    def _L0_cond_ref(Efou, y, weight):
        import jax, jax.numpy as jnp
        import numpy as np
        IN_FEATURES = 512
        OUT_FEATURES = 512
        BATCH = 32
        SEQ = 512
        EPS = 1e-08
        scale = 1.0 / np.sqrt(np.float32(weight.shape[0]))
        ys = y * scale
        d = jax.lax.rsqrt(jnp.einsum('bi,io->bo', ys * ys, weight * weight) + EPS)
        out = jnp.einsum('bsi,io->bso', Efou * ys[:, None, :], weight) * d[:, None, :]
        return out

    def _L1_cond_ref(x, h0, Wx, Wh, b):
        import jax, jax.numpy as jnp
        import numpy as np
        import math
        N, T, D, H = (128, 256, 512, 512)
        xw = jnp.einsum('ntd,dh->nth', x, Wx) + b

        def step(h_prev, xw_t):
            h_next = jnp.tanh(xw_t + h_prev @ Wh)
            return (h_next, h_next)
        _, hs = jax.lax.scan(step, h0, jnp.swapaxes(xw, 0, 1))
        return jnp.swapaxes(hs, 0, 1)
    x = x + _L0_cond_ref(x, cond_1024, L0_cond_weight)
    x = x + _L1_cond_ref(x, cond_1024, L1_cond_Wx, L1_cond_Wh, L1_cond_b)
    return x

_drawn_inputs = setup_inputs


def setup_inputs(seed=0):
    import zlib

    import numpy as np

    out = dict(_drawn_inputs(seed))
    spreads = {'L1_cond_b': (0.0, 0.1)}
    factors = {}
    for name, (base, spread) in spreads.items():
        noise = np.random.default_rng([zlib.crc32(name.encode()), seed]).standard_normal(out[name].shape)
        drawn = base * np.exp(spread * noise) if base else spread * noise
        out[name] = jnp.asarray(drawn.astype(out[name].dtype))
    for name, factor in factors.items():
        out[name] = (out[name] * factor).astype(out[name].dtype)
    return out
```

```python
from contextlib import ExitStack

import concourse.bass as bass
from concourse import mybir

FP32 = mybir.dt.float32
FP32R = mybir.dt.float32r
FP16 = mybir.dt.float16
I32 = mybir.dt.int32
ALU = mybir.AluOpType
ACT = mybir.ActivationFunctionType
AX = mybir.AxisListType

P = 128
EPS = 1e-8
LO = 1024.0
STEPS = 16
GROUP = 4
NG = STEPS // GROUP
STAGES = 3


def cond_resid_kernel(nc, x, cond, w0, wx, wh, bias, out):
    B, SEQ, F = x.shape
    FC = F // P
    COLS = STEPS * B
    GCOLS = GROUP * B
    NBLK = SEQ // STEPS
    assert GCOLS == P and COLS == 512 and F == 512 and FC == 4
    YSCALE = float(1.0 / F ** 0.5)

    x_groups = x.rearrange("b (g t) f -> g t b f", t=GROUP)
    out_groups = out.rearrange("b (g t) f -> g t b f", t=GROUP)

    with ExitStack() as ctx:
        def sb(name, shape, dt=FP32):
            return ctx.enter_context(nc.sbuf_tensor(name, shape, dt))

        def pb(name, shape=(P, 512)):
            return ctx.enter_context(nc.psum_tensor(name, list(shape), FP32))

        def sem(name):
            return ctx.enter_context(nc.semaphore(name))

        w0_raw, wx_raw, wh_raw = (sb(n, [P, FC, F]) for n in ("w0_raw", "wx_raw", "wh_raw"))
        w0_hi, w0_lo, wx_hi, wx_lo = (sb(n, [P, FC, F], FP32R) for n in ("w0_hi", "w0_lo", "wx_hi", "wx_lo"))
        wh_hi, wh_lo = (sb(n, [P, FC, F], FP16) for n in ("wh_hi", "wh_lo"))
        bias_t = sb("bias_t", [P, FC])
        ident = sb("ident", [P, P])
        cond_rows = sb("cond_rows", [B, F])
        cond_t = sb("cond_t", [P, FC, B])
        ys_sq = sb("ys_sq", [P, FC, B])
        ys_cols = sb("ys_cols", [P, FC, GROUP, B])
        d_cols = sb("d_cols", [P, FC, STEPS, B])
        d_var, d_root, d_inv = (sb(n, [P, FC, B]) for n in ("d_var", "d_root", "d_inv"))
        wh_max, wh_max_all = sb("wh_max", [P, 1]), sb("wh_max_all", [P, 1])
        exps = sb("exps", [P, 3], I32)
        wh_up, wh_down, wh_down_lo = (sb(n, [P, 1]) for n in ("wh_up", "wh_down", "wh_down_lo"))

        x_rows = sb("x_rows", [P, NG, F])
        x_t = sb("x_t", [P, FC, COLS])
        xs = sb("xs", [P, NG, FC, GCOLS])
        xs_hi, xs_lo = (sb(n, [P, FC, COLS], FP32R) for n in ("xs_hi", "xs_lo"))
        zd = sb("zd", [P, 2, COLS])
        x1 = sb("x1", [P, 2, FC, COLS])
        x1_hi, x1_lo = (sb(n, [P, FC, COLS], FP32R) for n in ("x1_hi", "x1_lo"))
        xw = sb("xw", [P, 2, FC, COLS])
        pre_hi, pre = sb("pre_hi", [P, FC, B]), sb("pre", [P, FC, B])
        h_parts = sb("h_parts", [P, FC, 2, B], FP16)
        lo_sum = sb("lo_sum", [P, 1])
        act_warm = sb("act_warm", [P, FC])
        y_t = sb("y_t", [P, 2, FC, GCOLS])
        y_rows = sb("y_rows", [P, 2, F])

        rec_ps = pb("rec_ps", (P, FC, 2, 64))
        rec_ps = rec_ps[:, :, :, 0:B]
        h_ps = [pb(f"h_ps{i}") for i in range(2)]
        mm_ps = [pb(f"mm_ps{i}") for i in range(2)]
        in_ps = [pb(f"in_ps{i}") for i in range(2)]
        out_ps = pb("out_ps")

        weights_in = {n: sem(f"{n}_in") for n in ("w0", "wx", "wh", "cond", "bias")}
        x_loaded = [sem(f"x_loaded{g}") for g in range(NG)]
        stored = [sem(f"stored{k}") for k in range(2)]
        ident_zero, ident_ready = sem("ident_zero"), sem("ident_ready")
        setup_pe, setup_dve, setup_act, setup_pool = (sem(f"setup_{n}") for n in ("pe", "dve", "act", "pool"))
        x_turned, x_t_ready, xs_ready, xs_hi_ready, xs_lo_ready = (
            sem(n) for n in ("x_turned", "x_t_ready", "xs_ready", "xs_hi_ready", "xs_lo_ready"))
        z_done, zd_ready, x1_ready, x1_hi_ready, x1_lo_ready = (
            sem(n) for n in ("z_done", "zd_ready", "x1_ready", "x1_hi_ready", "x1_lo_ready"))
        xw_done, xw_ready = sem("xw_done"), sem("xw_ready")
        rec_done, pre_part, pre_ready, h_hi_ready, h_ready, h_lo_ready = (
            sem(n) for n in ("rec_done", "pre_part", "pre_ready", "h_hi_ready", "h_ready", "h_lo_ready"))
        h_seen = sem("h_seen")
        y_ready, y_turned, y_rows_ready = sem("y_ready"), sem("y_turned"), sem("y_rows_ready")

        FIRST, LOOP_FROM, LOOP_TO = -2, 2, NBLK - 2
        assert (LOOP_TO - LOOP_FROM) % 2 == 0

        def run_blocks(engine, block_body, pairs):
            for i in range(FIRST, LOOP_FROM):
                block_body(i, i >= 0, i >= -1, True, i % 2)
            if pairs:
                with engine.Fori(0, (LOOP_TO - LOOP_FROM) // 2) as j:
                    for parity in range(2):
                        block_body(j * 2 + (LOOP_FROM + parity), True, True, True, parity)
            else:
                with engine.Fori(LOOP_FROM, LOOP_TO) as i:
                    block_body(i, True, True, True, None)
            for i in range(LOOP_TO, NBLK):
                block_body(i, True, i + 1 < NBLK, i + 2 < NBLK, i % 2)

        DVE_WH_MAX, DVE_COND_T, DVE_W_SQ, DVE_YS, DVE_D_VAR, DVE_D_READY, DVE_WEIGHTS = range(1, 8)

        TURN_IN_AT = {9: 0, 10: 1, 11: 2, 13: 3}
        XS_HIGH_AT = {10: (0,), 12: (1, 2), 14: (3,)}
        SCALE_OUT_AT = {1: 0, 3: 1, 5: 2, 7: 3}
        X1_HIGH_AT = {2: 0, 4: 1, 6: 2, 8: 3}
        XW_OUT_AT = {10: 0, 11: 1, 13: 2, 15: 3}

        block = ctx.enter_context(nc.Block())

        @block.sync
        def _(sp):
            def load(n, g, after=None):
                if after is not None:
                    sp.wait_ge(x_turned, after)
                sp.dma_start(x_rows[:, g, :], x_groups[n * NG + g]).then_inc(x_loaded[g], 16)

            def store(G, slot):
                sp.wait_ge(y_rows_ready, G + 1)
                sp.dma_start(out_groups[G], y_rows[:, slot, :]).then_inc(stored[slot], 16)

            sp.dma_start(cond_rows[:], cond).then_inc(weights_in["cond"], 16)
            load(0, 0)
            sp.dma_start(w0_raw[:], w0.rearrange("(c p) n -> p c n", p=P)).then_inc(weights_in["w0"], 16)
            for g in range(1, NG):
                load(0, g)
            sp.dma_start(wh_raw[:], wh.rearrange("(c p) n -> p c n", p=P)).then_inc(weights_in["wh"], 16)
            sp.dma_start(wx_raw[:], wx.rearrange("(c p) n -> p c n", p=P)).then_inc(weights_in["wx"], 16)
            with nc.allow_non_contiguous_dma(reason="512 values of the bias, once"):
                sp.dma_start(bias_t[:], bias.rearrange("(c p) -> p c", p=P)).then_inc(weights_in["bias"], 16)

            def block_body(i, rec, prod, load_stage, parity):
                first = isinstance(i, int) and i == 0
                more = load_stage and not (isinstance(i, int) and i + 3 >= NBLK)
                if rec and not first:
                    store(i * NG - 1, 1)
                if rec:
                    store(i * NG, 0)
                if more:
                    load(i + 3, 0, (i + 2) * NG + 1)
                    load(i + 3, 1, (i + 2) * NG + 2)
                if rec:
                    store(i * NG + 1, 1)
                if more:
                    load(i + 3, 2, (i + 2) * NG + 3)
                    load(i + 3, 3, (i + 2) * NG + 4)
                if rec:
                    store(i * NG + 2, 0)

            for i in range(FIRST, LOOP_FROM):
                block_body(i, i >= 0, True, True, None)
            with sp.Fori(LOOP_FROM, NBLK - STAGES) as i:
                block_body(i, True, True, True, None)
            for i in range(NBLK - STAGES, NBLK):
                block_body(i, True, True, False, None)
            store(NBLK * NG - 1, 1)
            for slot in range(2):
                sp.wait_ge(stored[slot], 16 * (NBLK * NG // 2))

        @block.gpsimd
        def _(pool):
            g = nc.gpsimd
            g.memset(ident[:], 0.0).then_inc(ident_zero, 1)
            pool.wait_ge(ident_zero, 1)
            g.affine_select(out=ident[:], in_=ident[:], compare_op=ALU.not_equal, fill=1.0, base=0,
                            pattern=[[-1, P]], channel_multiplier=1).then_inc(ident_ready, 1)
            pool.wait_ge(setup_dve, DVE_WH_MAX)
            g.partition_all_reduce(wh_max_all[:], wh_max[:], P, bass.bass_isa.ReduceOp.max).then_inc(setup_pool, 1)

            def xs_low(n, grp):
                pool.wait_ge(xs_hi_ready, n * NG + grp + 1)
                cols = slice(grp * GCOLS, (grp + 1) * GCOLS)
                g.tensor_tensor(xs_lo[:, :, cols], xs[:, grp], xs_hi[:, :, cols].bitcast(FP32),
                                ALU.subtract).then_inc(xs_lo_ready, 1)

            def x1_sum(n, m, par):
                pool.wait_ge(zd_ready, n * FC + m + 1)
                if m == 0:
                    pool.wait_ge(x_t_ready, n * NG + NG)
                g.tensor_tensor(x1[:, par, m, :], zd[:, m % 2, :], x_t[:, m, :], ALU.add).then_inc(x1_ready, 1)

            def x1_low(n, m, par):
                pool.wait_ge(x1_hi_ready, n * FC + m + 1)
                g.tensor_tensor(x1_lo[:, m, :], x1[:, par, m, :], x1_hi[:, m, :].bitcast(FP32),
                                ALU.subtract).then_inc(x1_lo_ready, 1)

            def block_body(i, rec, prod, load_stage, par):
                if prod:
                    for m in range(FC):
                        x1_sum(i + 1, m, 1 - par)
                        x1_low(i + 1, m, 1 - par)
                if load_stage:
                    for grp in range(NG):
                        xs_low(i + 2, grp)

            run_blocks(pool, block_body, True)

        @block.vector
        def _(dve):
            v = nc.vector
            chain = ctx.enter_context(nc.semaphore("dve_chain"))
            done = [0]

            def link(ins):
                done[0] += 1
                ins.then_inc(chain, 1)
                dve.wait_ge(chain, done[0])

            v.memset(h_parts[:], 0.0).then_inc(h_hi_ready, 1)
            dve.wait_ge(weights_in["wh"], 16)
            v.tensor_reduce(wh_max[:], wh_raw[:].rearrange("p c n -> p (c n)"), AX.X, ALU.max,
                            apply_absolute_value=True).then_inc(setup_dve, 1)
            dve.wait_ge(setup_pe, 1)
            v.tensor_copy(cond_t[:].rearrange("p c b -> p (c b)"), out_ps[:, 0:FC * B]).then_inc(setup_dve, 1)
            dve.wait_ge(weights_in["w0"], 16)
            w_sq = x1[:, 0]
            v.tensor_tensor(w_sq, w0_raw[:], w0_raw[:], ALU.mult).then_inc(setup_dve, 1)
            dve.wait_ge(setup_dve, DVE_COND_T)
            for t in range(GROUP):
                last = v.tensor_scalar(ys_cols[:, :, t, :], cond_t[:], YSCALE, None, ALU.mult)
            link(last)
            v.tensor_tensor(ys_sq[:], ys_cols[:, :, 0, :], ys_cols[:, :, 0, :], ALU.mult).then_inc(setup_dve, 1)
            link(v.tensor_copy(w0_hi[:], w0_raw[:]))
            v.tensor_tensor(w0_lo[:], w0_raw[:], w0_hi[:].bitcast(FP32), ALU.subtract)
            dve.wait_ge(setup_pe, 2)
            v.tensor_scalar(d_var[:].rearrange("p c b -> p (c b)"), out_ps[:, 0:FC * B], EPS, None,
                            ALU.add).then_inc(setup_dve, 1)
            dve.wait_ge(setup_act, 1)
            link(v.reciprocal(d_inv[:], d_root[:]))
            link(v.tensor_tensor(d_var[:], d_var[:], d_inv[:], ALU.mult))
            link(v.tensor_tensor(d_var[:], d_var[:], d_inv[:], ALU.mult))
            link(v.tensor_scalar(d_var[:], d_var[:], -0.5, 1.5, ALU.mult, ALU.add))
            for t in range(STEPS):
                last = v.tensor_tensor(d_cols[:, :, t, :], d_var[:], d_inv[:], ALU.mult)
            last.then_inc(setup_dve, 1)
            dve.wait_ge(setup_dve, DVE_D_READY)
            dve.wait_ge(weights_in["wx"], 16)
            link(v.tensor_copy(wx_hi[:], wx_raw[:]))
            v.tensor_tensor(wx_lo[:], wx_raw[:], wx_hi[:].bitcast(FP32), ALU.subtract)
            dve.wait_ge(setup_pool, 1)
            link(v.tensor_single_scalar(exps[:, 0:1], wh_max_all[:].bitcast(I32), 23, op=ALU.logical_shift_right))
            link(v.tensor_scalar(exps[:, 0:1], exps[:, 0:1], 32.0, None, ALU.max))
            link(v.tensor_scalar(exps[:, 1:2], exps[:, 0:1], -1.0, 268.0, ALU.mult, ALU.add))
            link(v.tensor_scalar(exps[:, 2:3], exps[:, 0:1], -14.0, None, ALU.add))
            link(v.tensor_single_scalar(wh_up[:].bitcast(I32), exps[:, 1:2], 23, op=ALU.logical_shift_left))
            link(v.tensor_single_scalar(wh_down[:].bitcast(I32), exps[:, 2:3], 23, op=ALU.logical_shift_left))
            link(v.tensor_scalar(wh_down_lo[:], wh_down[:], 1.0 / LO, None, ALU.mult))
            wh_scaled = wx_raw
            link(v.tensor_scalar(wh_scaled[:], wh_raw[:], wh_up[:], None, ALU.mult))
            link(v.tensor_copy(wh_hi[:], wh_scaled[:]))
            link(v.tensor_tensor(wh_scaled[:], wh_scaled[:], wh_hi[:], ALU.subtract))
            v.tensor_scalar(wh_lo[:], wh_scaled[:], LO, None, ALU.mult).then_inc(setup_dve, 1)

            def scale_in(n, grp):
                dve.wait_ge(x_t_ready, n * NG + grp + 1)
                if not i_is(n, 0):
                    dve.wait_ge(xs_lo_ready, (n - 1) * NG + grp + 1)
                v.tensor_tensor(xs[:, grp].rearrange("p c k -> p (c k)"), in_ps[grp % 2][:],
                                ys_cols[:].rearrange("p c t b -> p (c t b)"), ALU.mult).then_inc(xs_ready, 1)

            def scale_out(n, m):
                dve.wait_ge(z_done, n * FC + m + 1)
                if not (isinstance(n, int) and n == 0 and m < 2):
                    dve.wait_ge(x1_ready, n * FC + m - 1)
                v.tensor_tensor(zd[:, m % 2, :], mm_ps[m % 2][:],
                                d_cols[:, m].rearrange("p t b -> p (t b)"), ALU.mult).then_inc(zd_ready, 1)

            def sum_out(bank, grp, par):
                v.tensor_tensor(y_t[:, bank], h_ps[bank][:].rearrange("p (c k) -> p c k", c=FC),
                                x1[:, par, :, grp * GCOLS:(grp + 1) * GCOLS], ALU.add).then_inc(y_ready, 1)

            def step(i, s, par):
                n = i * STEPS + s
                if s == 0:
                    dve.wait_ge(xw_ready, i * FC + FC)
                dve.wait_ge(rec_done, n + 1)
                v.scalar_tensor_tensor(out=pre_hi[:], in0=rec_ps[:, :, 0, :], scalar=wh_down[:],
                                       in1=xw[:, par, :, s * B:(s + 1) * B], op0=ALU.mult,
                                       op1=ALU.add).then_inc(pre_part, 1)
                dve.wait_ge(pre_part, n + 1)
                v.scalar_tensor_tensor(out=pre[:], in0=rec_ps[:, :, 1, :], scalar=wh_down_lo[:], in1=pre_hi[:],
                                       op0=ALU.mult, op1=ALU.add).then_inc(pre_ready, 1)
                grp, t = s // GROUP, s % GROUP
                dve.wait_ge(h_ready, n + 1).then_inc(h_seen, 1)
                h_now = h_ps[grp % 2][:].rearrange("p (c t b) -> p c t b", c=FC, t=GROUP)[:, :, t, :]
                v.tensor_tensor_reduce(out=h_parts[:, :, 1, :], in0=h_now, in1=h_parts[:, :, 0, :], scale=LO,
                                       scalar=0.0, op0=ALU.subtract, op1=ALU.max,
                                       accum_out=lo_sum[:]).then_inc(h_lo_ready, 1)

            def block_body(i, rec, prod, load_stage, par):
                for s in range(STEPS):
                    if rec:
                        step(i, s, par)
                        if s % GROUP == 0 and not (i_is(i, 0) and s == 0):
                            grp = (s // GROUP - 1) % NG
                            sum_out(grp % 2, grp, par if s else 1 - par)
                    if prod and s in SCALE_OUT_AT:
                        scale_out(i + 1, SCALE_OUT_AT[s])
                    if load_stage and s in TURN_IN_AT:
                        scale_in(i + 2, TURN_IN_AT[s])
                    if i_is(i, -2) and s == STEPS - 1:
                        pass
                if i_is(i, -1):
                    dve.wait_ge(xw_ready, FC)
                    dve.wait_ge(setup_pe, 3)
                    link(v.tensor_tensor(xw[:, 0, :, 0:B], out_ps[:, 0:FC * B].rearrange("p (c b) -> p c b", c=FC),
                                         xw[:, 0, :, 0:B], ALU.add))

            run_blocks(dve, block_body, True)
            sum_out((NG - 1) % 2, NG - 1, (NBLK - 1) % 2)

        @block.scalar
        def _(act):
            a = nc.scalar
            act.wait_ge(setup_dve, DVE_D_VAR)
            a.activation(d_root[:], d_var[:], ACT.Sqrt).then_inc(setup_act, 1)
            act.wait_ge(weights_in["bias"], 16)
            a.activation(act_warm[:], bias_t[:], ACT.Tanh)

            def copy_in(n, grp):
                act.wait_ge(x_turned, n * NG + grp + 1)
                if grp == 0 and not i_is(n, 0):
                    act.wait_ge(x1_ready, n * FC)
                a.activation(x_t[:, :, grp * GCOLS:(grp + 1) * GCOLS],
                             in_ps[grp % 2][:].rearrange("p (c k) -> p c k", c=FC), ACT.Copy).then_inc(x_t_ready, 1)

            def xs_high(n, grp):
                act.wait_ge(xs_ready, n * NG + grp + 1)
                if grp == 0 and not i_is(n, 0):
                    act.wait_ge(z_done, n * FC)
                a.activation(xs_hi[:, :, grp * GCOLS:(grp + 1) * GCOLS], xs[:, grp], ACT.Copy).then_inc(xs_hi_ready, 1)

            def x1_high(n, m, par):
                act.wait_ge(x1_ready, n * FC + m + 1)
                if m == 0 and not i_is(n, 0):
                    act.wait_ge(xw_done, n * FC)
                a.activation(x1_hi[:, m, :], x1[:, par, m, :], ACT.Copy).then_inc(x1_hi_ready, 1)

            def xw_out(n, m, par):
                act.wait_ge(xw_done, n * FC + m + 1)
                a.activation(xw[:, par, m, :], mm_ps[m % 2][:], ACT.Identity, bias=bias_t[:, m:m + 1]).then_inc(xw_ready, 1)

            def rows_out(G, slot, wait_store):
                act.wait_ge(y_turned, G + 1)
                if wait_store is not None:
                    act.wait_ge(stored[slot], wait_store)
                a.activation(y_rows[:, slot, :], out_ps[:], ACT.Copy).then_inc(y_rows_ready, 1)

            def step(i, s):
                grp, t = s // GROUP, s % GROUP
                n = i * STEPS + s
                act.wait_ge(pre_ready, n + 1)
                a.activation(h_parts[:, :, 0, :], pre[:], ACT.Tanh).then_inc(h_hi_ready, 1)
                h_now = h_ps[grp % 2][:].rearrange("p (c t b) -> p c t b", c=FC, t=GROUP)[:, :, t, :]
                a.activation(h_now, pre[:], ACT.Tanh).then_inc(h_ready, 1)

            def turned_rows(i, s):
                k = (s - 2) // GROUP - 1
                G = i * NG + k
                slot = k % 2
                if k < 0:
                    stores = i * (NG // 2) - 1
                elif k == 0:
                    stores = i * (NG // 2)
                elif k == 1:
                    stores = i * (NG // 2)
                else:
                    stores = i * (NG // 2) + 1
                skip = isinstance(i, int) and stores <= 0
                rows_out(G, slot, None if skip else stores * 16)

            def block_body(i, rec, prod, load_stage, par):
                for s in range(STEPS):
                    if rec:
                        step(i, s)
                        if s % GROUP == 2 and not (i_is(i, 0) and s == 2):
                            turned_rows(i, s)
                    if prod:
                        if s in X1_HIGH_AT:
                            x1_high(i + 1, X1_HIGH_AT[s], 1 - par)
                        if s in XW_OUT_AT:
                            xw_out(i + 1, XW_OUT_AT[s], 1 - par)
                    if load_stage and s in TURN_IN_AT:
                        copy_in(i + 2, TURN_IN_AT[s])
                    if load_stage:
                        for grp in XS_HIGH_AT.get(s, ()):
                            xs_high(i + 2, grp)

            run_blocks(act, block_body, True)
            rows_out(NBLK * NG - 1, 1, 16 * (NBLK * NG // 2 - 1))

        @block.tensor
        def _(pe):
            mm = nc.tensor.matmul
            pe.wait_ge(ident_ready, 1)
            pe.wait_ge(weights_in["cond"], 16)
            for c in range(FC):
                last = nc.tensor.transpose(out_ps[:, c * B:(c + 1) * B], cond_rows[:, c * P:(c + 1) * P], ident[0:B, 0:B])
            last.then_inc(setup_pe, 1)
            pe.wait_ge(setup_dve, DVE_YS)
            w_sq = x1[:, 0]
            for m in range(FC):
                for k in range(FC):
                    last = mm(out_ps[:, m * B:(m + 1) * B], w_sq[:, k, m * P:(m + 1) * P], ys_sq[:, k, :],
                              start=(k == 0), stop=(k == FC - 1))
            last.then_inc(setup_pe, 1)

            def turn_in(n, grp):
                pe.wait_ge(x_loaded[grp], (n + 1) * 16)
                if not (isinstance(n, int) and n == 0 and grp < 2):
                    pe.wait_ge(xs_ready, n * NG + grp - 1)
                for c in range(FC):
                    last = nc.tensor.transpose(in_ps[grp % 2][:, c * P:(c + 1) * P],
                                               x_rows[:, grp, c * P:(c + 1) * P], ident[:])
                last.then_inc(x_turned, 1)

            def product(bank, w_h, w_l, v_h, v_l, m, ks):
                for k in ks:
                    cols = slice(m * P, (m + 1) * P)
                    mm(bank[:], w_l[:, k, cols], v_h[:, k, :], start=(k == 0), stop=False)
                    mm(bank[:], w_h[:, k, cols], v_h[:, k, :], start=False, stop=False)
                    last = mm(bank[:], w_h[:, k, cols], v_l[:, k, :], start=False, stop=(k == FC - 1))
                return last

            def layer0_unit(n, u):
                m, half = u // 2, u % 2
                if u == 0:
                    pe.wait_ge(xs_hi_ready, n * NG + NG)
                    pe.wait_ge(xs_lo_ready, n * NG + NG)
                    if not i_is(n, 0):
                        pe.wait_ge(xw_ready, n * FC)
                if half == 0 and m >= 2:
                    pe.wait_ge(zd_ready, n * FC + m - 1)
                last = product(mm_ps[m % 2], w0_hi, w0_lo, xs_hi, xs_lo, m, (2 * half, 2 * half + 1))
                if half:
                    last.then_inc(z_done, 1)

            def layer1_unit(n, u):
                m, half = ((0, 0), (1, 0), (0, 1), (1, 1), (2, 0), (2, 1), (3, 0), (3, 1))[u]
                if half == 0 and m < 2:
                    pe.wait_ge(zd_ready, n * FC + 3 + m)
                if half == 0 and m >= 2:
                    pe.wait_ge(xw_ready, n * FC + m - 1)
                if u in (0, 2):
                    pe.wait_ge(x1_hi_ready, n * FC + 2 + u)
                    pe.wait_ge(x1_lo_ready, n * FC + 2 + u)
                last = product(mm_ps[m % 2], wx_hi, wx_lo, x1_hi, x1_lo, m, (2 * half, 2 * half + 1))
                if half:
                    last.then_inc(xw_done, 1)

            def step(i, s):
                n = i * STEPS + s
                pe.wait_ge(h_hi_ready, n + 1)
                for m in range(FC):
                    for k in range(FC):
                        mm(rec_ps[:, m, 1, :], wh_lo[:, k, m * P:(m + 1) * P], h_parts[:, k, 0, :],
                           start=(m == 0 and k == 0), stop=False, skip_group_check=True)
                if not i_is(n, 0):
                    pe.wait_ge(h_lo_ready, n)
                for m in range(FC):
                    for k in range(FC):
                        last = mm(rec_ps[:, m, :, :], wh_hi[:, k, m * P:(m + 1) * P], h_parts[:, k, :, :],
                                  start=False, stop=(m == FC - 1 and k == FC - 1), skip_group_check=True)
                last.then_inc(rec_done, 1)

            def turn_out(G, bank):
                pe.wait_ge(y_ready, G + 1)
                if not i_is(G, 0):
                    pe.wait_ge(y_rows_ready, G)
                for c in range(FC):
                    last = nc.tensor.transpose(out_ps[:, c * P:(c + 1) * P], y_t[:, bank, c, :], ident[:])
                last.then_inc(y_turned, 1)

            def block_body(i, rec, prod, load_stage, par):
                if i_is(i, -1):
                    pe.wait_ge(setup_dve, DVE_WEIGHTS)
                for s in range(STEPS):
                    if rec:
                        step(i, s)
                        if s % GROUP == 1 and not (i_is(i, 0) and s == 1):
                            k = (s - 1) // GROUP - 1
                            turn_out(i * NG + k, k % 2)
                    if prod and s < 8:
                        layer0_unit(i + 1, s)
                    if load_stage and s in TURN_IN_AT:
                        turn_in(i + 2, TURN_IN_AT[s])
                    if prod and s >= 8:
                        layer1_unit(i + 1, s - 8)
                if i_is(i, -1):
                    for m in range(FC):
                        for k in range(FC):
                            last = mm(out_ps[:, m * B:(m + 1) * B], wh_raw[:, k, m * P:(m + 1) * P],
                                      cond_t[:, k, :], start=(k == 0), stop=(k == FC - 1))
                    last.then_inc(setup_pe, 1)

            run_blocks(pe, block_body, False)
            turn_out(NBLK * NG - 1, 1)


def i_is(value, number):
    return isinstance(value, int) and value == number


_INS = ["x", "cond_1024", "L0_cond_weight", "L1_cond_Wx", "L1_cond_Wh", "L1_cond_b"]


def kernel(**inputs):
    import numpy as np
    import concourse.bacc as bacc
    from concourse.bass_utils import run_bass_kernel_spmd

    nc = bacc.Bacc("TRN2", target_bir_lowering=False, num_devices=1)
    arrays, args = {}, []
    for name in _INS:
        a = np.ascontiguousarray(inputs[name])
        arrays[f"in_{name}_dram"] = a
        args.append(nc.dram_tensor(f"in_{name}_dram", a.shape, mybir.dt.from_np(a.dtype), kind="ExternalInput").ap())
    shape = inputs["x"].shape
    out = nc.dram_tensor("out_dram", shape, FP32, kind="ExternalOutput").ap()
    cond_resid_kernel(nc, *args, out)
    r = run_bass_kernel_spmd(nc, [arrays], core_ids=[0])
    return r.results[0]["out_dram"]
```

```python
from contextlib import ExitStack

import concourse.bass as bass
from concourse import mybir

FP32 = mybir.dt.float32
FP32R = mybir.dt.float32r
FP16 = mybir.dt.float16
I32 = mybir.dt.int32
ALU = mybir.AluOpType
ACT = mybir.ActivationFunctionType
AX = mybir.AxisListType

P = 128
SQ = 32
EPS = 1e-8
LO = 1024.0
STEPS = 16
GROUP = 4
NG = STEPS // GROUP
STAGES = 3


def i_is(value, number):
    return isinstance(value, int) and value == number


def cond_resid_kernel(nc, x, cond, w0, wx, wh, bias, out):
    B, SEQ, F = x.shape
    FC = F // P
    NQ = P // SQ
    COLS = STEPS * B
    GCOLS = GROUP * B
    NBLK = SEQ // STEPS
    assert B == SQ and COLS == 512 and F == NQ * P and FC == NQ
    YSCALE = float(1.0 / F ** 0.5)
    HALVES = (slice(0, FC // 2), slice(FC // 2, FC))

    PAIR = 2 * GROUP
    x_blocks = x.rearrange("b (i t) (q n) -> i q b t n", t=STEPS, q=NQ)
    out_pairs = out.rearrange("b (j t) (q n) -> j q b t n", t=PAIR, q=NQ)

    with ExitStack() as ctx:
        def sb(name, shape, dt=FP32):
            return ctx.enter_context(nc.sbuf_tensor(name, shape, dt))

        def pb(name, shape=(P, 512)):
            return ctx.enter_context(nc.psum_tensor(name, list(shape), FP32))

        def sem(name):
            return ctx.enter_context(nc.semaphore(name))

        w0_raw, wx_raw, wh_raw = (sb(n, [P, FC, F]) for n in ("w0_raw", "wx_raw", "wh_raw"))
        w0_hi, w0_lo, wx_hi, wx_lo = (sb(n, [P, FC, F], FP32R) for n in ("w0_hi", "w0_lo", "wx_hi", "wx_lo"))
        wh_hi, wh_lo = (sb(n, [P, FC, F], FP16) for n in ("wh_hi", "wh_lo"))

        def raw_chunks(w, k):
            return w[:, k, :].rearrange("p (q m f) -> p m q f", q=NQ, m=FC)

        def part_chunks(w, k):
            return w[:, k, :].rearrange("p (m q f) -> p m q f", q=NQ, m=FC)

        bias_t = sb("bias_t", [P, FC])
        cond_rows = sb("cond_rows", [P, P])
        cond_t = sb("cond_t", [P, FC, B])
        ys_sq = sb("ys_sq", [P, FC, B])
        ys_cols = sb("ys_cols", [P, FC, GROUP, B])
        d_cols = sb("d_cols", [P, FC, STEPS, B])
        d_var, d_root, d_inv = (sb(n, [P, FC, B]) for n in ("d_var", "d_root", "d_inv"))
        wh_max, wh_max_all = sb("wh_max", [P, 1]), sb("wh_max_all", [P, 1])
        exps = sb("exps", [P, 3], I32)
        wh_up, wh_down, wh_down_lo = (sb(n, [P, 1]) for n in ("wh_up", "wh_down", "wh_down_lo"))
        table_warm = sb("table_warm", [P, FC])

        x_rows = sb("x_rows", [P, STEPS, FC, SQ])
        x_t = sb("x_t", [P, 2, FC, STEPS, B])
        xs = sb("xs", [P, NG, FC, GCOLS])
        xs_hi, xs_lo = (sb(n, [P, FC, COLS], FP32R) for n in ("xs_hi", "xs_lo"))
        zd = sb("zd", [P, 2, COLS])
        x1 = sb("x1", [P, 2, FC, COLS])
        x1_hi, x1_lo = (sb(n, [P, FC, COLS], FP32R) for n in ("x1_hi", "x1_lo"))
        xw = sb("xw", [P, 2, FC, COLS])
        pre_hi, pre = sb("pre_hi", [P, FC, B]), sb("pre", [P, FC, B])
        h_parts = sb("h_parts", [P, FC, 2, B], FP16)
        lo_max = sb("lo_max", [P, 2])
        y_t = sb("y_t", [P, 2, FC, GROUP, B])
        y_rows = sb("y_rows", [P, STEPS, FC, SQ])
        w_sq, wh_cols = x1[:, 0], x1[:, 1]

        rec_ps = [pb(f"rec_ps{i}", (P, FC // 2, 2, P)) for i in range(2)]
        h_ps = pb("h_ps", (P, FC, 2 * GROUP, B))
        mm_ps = [pb(f"mm_ps{i}") for i in range(4)]
        setup_ps = h_ps[:, :, 0, :]

        w0_in, wx_in, wh_in, cond_in, bias_in = (sem(n) for n in ("w0_in", "wx_in", "wh_in", "cond_in", "bias_in"))
        x_loaded = sem("x_loaded")
        stored = [sem(f"stored{k}") for k in range(2)]
        cond_ready, ys_sq_ready, w_sq_ready, d_var_ready, d_root_ready, d_ready = (
            sem(n) for n in ("cond_ready", "ys_sq_ready", "w_sq_ready", "d_var_ready", "d_root_ready", "d_ready"))
        var_done, first_done, max_ready, max_all_ready = (
            sem(n) for n in ("var_done", "first_done", "max_ready", "max_all_ready"))
        w0_hi_ready, w0_ready, wx_hi_ready, wx_ready, wh_cols_ready, wh_ready, dve_done = (
            sem(n) for n in ("w0_hi_ready", "w0_ready", "wx_hi_ready", "wx_ready", "wh_cols_ready", "wh_ready", "dve_done"))
        x_turned, xs_ready, xs_hi_ready, xs_lo_ready = (
            sem(n) for n in ("x_turned", "xs_ready", "xs_hi_ready", "xs_lo_ready"))
        z_done, zd_ready, x1_ready, x1_hi_ready, x1_lo_ready = (
            sem(n) for n in ("z_done", "zd_ready", "x1_ready", "x1_hi_ready", "x1_lo_ready"))
        xw_done, xw_ready = sem("xw_done"), sem("xw_ready")
        rec_done, pre_part, pre_ready, h_hi_ready, h_ready, h_seen, h_lo_ready = (
            [sem(f"{n}{i}") for i in range(2)] for n in ("rec_done", "pre_part", "pre_ready", "h_hi_ready", "h_ready",
                                                         "h_seen", "h_lo_ready"))
        y_ready, y_rows_ready = sem("y_ready"), sem("y_rows_ready")

        FIRST, LOOP_FROM, LOOP_TO = -2, 2, NBLK - 2
        assert LOOP_FROM % 2 == 0 and (LOOP_TO - LOOP_FROM) % 2 == 0

        def run_blocks(engine, block_body, pairs):
            for i in range(FIRST, LOOP_FROM):
                block_body(i, i >= 0, i >= -1, True, i % 2)
            if pairs:
                with engine.Fori(0, (LOOP_TO - LOOP_FROM) // 2) as j:
                    for parity in range(2):
                        block_body(j * 2 + (LOOP_FROM + parity), True, True, True, parity)
            else:
                with engine.Fori(LOOP_FROM, LOOP_TO) as i:
                    block_body(i, True, True, True, None)
            for i in range(LOOP_TO, NBLK):
                block_body(i, True, i + 1 < NBLK, i + 2 < NBLK, i % 2)

        TURN_OUT_AT = {1: 3, 7: 0, 10: 1, 13: 2}
        SCALE_OUT_AT = {2: 0, 4: 1, 6: 2, 8: 3}
        TURN_IN_AT = {3: 0, 9: 1, 11: 2, 12: 3}
        X1_HIGH_AT = {3: 0, 5: 1, 7: 2, 9: 3}
        XS_HIGH_AT = {8: 0, 11: 1, 13: 2, 14: 3}
        XW_OUT_AT = {12: 0, 13: 1, 14: 2, 15: 3}
        LAYER0_UNITS = [(m, half) for m in range(FC) for half in range(2)]
        LAYER1_UNITS = [(0, 0), (1, 0), (2, 0), (0, 1), (1, 1), (3, 0), (2, 1), (3, 1)]

        block = ctx.enter_context(nc.Block())

        @block.sync
        def _(sp):
            def quarter(q):
                return slice(q * SQ, (q + 1) * SQ)

            def load_weight(w_raw, w, loaded):
                rows = w.rearrange("(q c f) n -> q f c n", q=NQ, c=FC)
                for q in range(NQ):
                    sp.dma_start(w_raw[quarter(q)], rows[q]).then_inc(loaded, 16)

            def load(n):
                if not i_is(n, 0):
                    sp.wait_ge(x_turned, n * NG)
                for q in range(NQ):
                    sp.dma_start(x_rows[quarter(q)].rearrange("p t c f -> p t (c f)"), x_blocks[n, q]).then_inc(x_loaded, 16)

            def store(i, pair):
                sp.wait_ge(y_rows_ready, i * NG + 2 * pair + 2)
                for q in range(NQ):
                    sp.dma_start(out_pairs[i * 2 + pair, q],
                                 y_rows[quarter(q), pair * PAIR:(pair + 1) * PAIR].rearrange("p t c f -> p t (c f)")
                                 ).then_inc(stored[pair], 16)

            cond_quarters = cond.rearrange("b (q n) -> q b n", q=NQ)
            for q in range(NQ):
                sp.dma_start(cond_rows[quarter(q)], cond_quarters[q]).then_inc(cond_in, 16)
            load(0)
            load_weight(w0_raw, w0, w0_in)
            load_weight(wx_raw, wx, wx_in)
            load_weight(wh_raw, wh, wh_in)

            def block_body(i, load_next):
                if not i_is(i, 0):
                    store(i - 1, 1)
                if load_next:
                    load(i + 3)
                store(i, 0)

            load(1)
            load(2)
            for i in range(LOOP_FROM):
                block_body(i, True)
            with sp.Fori(LOOP_FROM, NBLK - STAGES) as i:
                block_body(i, True)
            for i in range(NBLK - STAGES, NBLK):
                block_body(i, False)
            store(NBLK - 1, 1)
            for pair in range(2):
                sp.wait_ge(stored[pair], NBLK * NQ * 16)

        @block.gpsimd
        def _(pool):
            g = nc.gpsimd

            def scale_in(n, grp, par):
                pool.wait_ge(x_turned, n * NG + grp + 1)
                g.tensor_tensor(xs[:, grp], x_t[:, par, :, grp * GROUP:(grp + 1) * GROUP, :].rearrange("p c t b -> p c (t b)"),
                                ys_cols[:].rearrange("p c t b -> p c (t b)"), ALU.mult).then_inc(xs_ready, 1)

            def xs_low(n, grp):
                pool.wait_ge(xs_hi_ready, n * NG + grp + 1)
                cols = slice(grp * GCOLS, (grp + 1) * GCOLS)
                g.tensor_tensor(xs_lo[:, :, cols], xs[:, grp], xs_hi[:, :, cols].bitcast(FP32),
                                ALU.subtract).then_inc(xs_lo_ready, 1)

            def x1_sum(n, m, par):
                pool.wait_ge(zd_ready, n * FC + m + 1)
                g.tensor_tensor(x1[:, par, m, :], zd[:, m % 2, :], x_t[:, par, m].rearrange("p t b -> p (t b)"),
                                ALU.add).then_inc(x1_ready, 1)

            def x1_low(n, m, par):
                pool.wait_ge(x1_hi_ready, n * FC + m + 1)
                g.tensor_tensor(x1_lo[:, m, :], x1[:, par, m, :], x1_hi[:, m, :].bitcast(FP32),
                                ALU.subtract).then_inc(x1_lo_ready, 1)

            def block_body(i, rec, prod, turn, par):
                if i_is(i, -1):
                    pool.wait_ge(wx_hi_ready, FC)
                    for k in range(FC):
                        g.tensor_tensor(part_chunks(wx_lo, k), raw_chunks(wx_raw, k),
                                        part_chunks(wx_hi, k).bitcast(FP32), ALU.subtract).then_inc(wx_ready, 1)
                    pool.wait_ge(max_ready, 1)
                    g.partition_all_reduce(wh_max_all[:], wh_max[:], P, bass.bass_isa.ReduceOp.max).then_inc(max_all_ready, 1)
                if prod:
                    x1_sum(i + 1, 0, 1 - par)
                if turn:
                    scale_in(i + 2, 0, par)
                if prod:
                    x1_low(i + 1, 0, 1 - par)
                    for m in (1, 2):
                        x1_sum(i + 1, m, 1 - par)
                        x1_low(i + 1, m, 1 - par)
                    x1_sum(i + 1, 3, 1 - par)
                    x1_low(i + 1, 3, 1 - par)
                if turn:
                    scale_in(i + 2, 1, par)
                    xs_low(i + 2, 0)
                    scale_in(i + 2, 2, par)
                    xs_low(i + 2, 1)
                    scale_in(i + 2, 3, par)
                    xs_low(i + 2, 2)
                    xs_low(i + 2, 3)

            pool.wait_ge(ys_sq_ready, 1)
            run_blocks(pool, block_body, True)

        @block.vector
        def _(dve):
            v = nc.vector
            done = [0]

            def link(ins):
                done[0] += 1
                ins.then_inc(dve_done, 1)
                dve.wait_ge(dve_done, done[0])

            v.memset(h_parts[:], 0.0).then_inc(h_hi_ready[0], 1)
            dve.wait_ge(cond_in, NQ * 16)
            v.transpose(cond_t[:], cond_rows[:].rearrange("p (c f) -> p c f", c=FC)).then_inc(cond_ready, 1)
            dve.wait_ge(cond_ready, 1)
            for t in range(GROUP):
                last = v.tensor_scalar(ys_cols[:, :, t, :], cond_t[:], YSCALE, None, ALU.mult)
            link(last)
            v.tensor_tensor(ys_sq[:], ys_cols[:, :, 0, :], ys_cols[:, :, 0, :], ALU.mult).then_inc(ys_sq_ready, 1)

            def setup_layer0():
                dve.wait_ge(w0_in, NQ * 16)
                for k in range(FC):
                    v.tensor_tensor(part_chunks(w_sq, k), raw_chunks(w0_raw, k), raw_chunks(w0_raw, k),
                                    ALU.mult).then_inc(w_sq_ready, 1)
                dve.wait_ge(w0_hi_ready, FC)
                for k in range(FC):
                    v.tensor_tensor(part_chunks(w0_lo, k), raw_chunks(w0_raw, k),
                                    part_chunks(w0_hi, k).bitcast(FP32), ALU.subtract).then_inc(w0_ready, 1)
                dve.wait_ge(var_done, 1)
                v.tensor_scalar(d_var[:], setup_ps, EPS, None, ALU.add).then_inc(d_var_ready, 1)
                dve.wait_ge(d_root_ready, 1)
                link(v.reciprocal(d_inv[:], d_root[:]))
                link(v.tensor_tensor(d_var[:], d_var[:], d_inv[:], ALU.mult))
                link(v.tensor_tensor(d_var[:], d_var[:], d_inv[:], ALU.mult))
                link(v.tensor_scalar(d_var[:], d_var[:], -0.5, 1.5, ALU.mult, ALU.add))
                link(v.tensor_tensor(d_var[:], d_var[:], d_inv[:], ALU.mult))
                for t in range(STEPS):
                    v.tensor_copy(d_cols[:, :, t, :], d_var[:]).then_inc(d_ready, 1)
                dve.wait_ge(wh_in, NQ * 16)
                v.tensor_reduce(wh_max[:], wh_raw[:].rearrange("p c n -> p (c n)"), AX.X, ALU.max,
                                apply_absolute_value=True).then_inc(max_ready, 1)
                dve.wait_ge(d_ready, STEPS)

            def setup_recurrence():
                dve.wait_ge(max_all_ready, 1)
                link(v.tensor_single_scalar(exps[:, 0:1], wh_max_all[:].bitcast(I32), 23, op=ALU.logical_shift_right))
                link(v.tensor_scalar(exps[:, 0:1], exps[:, 0:1], 32.0, None, ALU.max))
                link(v.tensor_scalar(exps[:, 1:2], exps[:, 0:1], -1.0, 268.0, ALU.mult, ALU.add))
                link(v.tensor_scalar(exps[:, 2:3], exps[:, 0:1], -14.0, None, ALU.add))
                link(v.tensor_single_scalar(wh_up[:].bitcast(I32), exps[:, 1:2], 23, op=ALU.logical_shift_left))
                link(v.tensor_single_scalar(wh_down[:].bitcast(I32), exps[:, 2:3], 23, op=ALU.logical_shift_left))
                link(v.tensor_scalar(wh_down_lo[:], wh_down[:], 1.0 / LO, None, ALU.mult))
                wh_scaled = w0_raw
                dve.wait_ge(wh_cols_ready, FC)
                link(v.tensor_scalar(wh_scaled[:], wh_cols, wh_up[:], None, ALU.mult))
                link(v.tensor_copy(wh_hi[:], wh_scaled[:]))
                link(v.tensor_tensor(wh_scaled[:], wh_scaled[:], wh_hi[:], ALU.subtract))
                v.tensor_scalar(wh_lo[:], wh_scaled[:], LO, None, ALU.mult).then_inc(wh_ready, 1)

            def turn_in(n, grp, par):
                if grp == 0:
                    dve.wait_ge(x_loaded, (n + 1) * (NQ * 16))
                v.transpose(x_t[:, par, :, grp * GROUP:(grp + 1) * GROUP, :].rearrange("p c t b -> p t c b"),
                            x_rows[:, grp * GROUP:(grp + 1) * GROUP]).then_inc(x_turned, 1)

            def scale_out(n, m):
                dve.wait_ge(z_done, n * FC + m + 1)
                if not (i_is(n, 0) and m < 2):
                    dve.wait_ge(x1_ready, n * FC + m - 1)
                v.tensor_tensor(zd[:, m % 2, :], mm_ps[m][:],
                                d_cols[:, m].rearrange("p t b -> p (t b)"), ALU.mult).then_inc(zd_ready, 1)

            def sum_out(grp, half, par):
                c, at = HALVES[half], grp % 2 * GROUP
                v.tensor_tensor(y_t[:, grp % 2, c], h_ps[:, c, at:at + GROUP, :],
                                x1[:, par, c, grp * GCOLS:(grp + 1) * GCOLS].rearrange("p c (t b) -> p c t b", t=GROUP),
                                ALU.add).then_inc(y_ready, 1)

            def turn_out(i, grp):
                dve.wait_ge(y_ready, (i * NG + grp + 1) * 2)
                if grp % 2 == 0 and not i_is(i, 0):
                    dve.wait_ge(stored[grp // 2], i * (NQ * 16))
                v.transpose(y_rows[:, grp * GROUP:(grp + 1) * GROUP], y_t[:, grp % 2].rearrange("p c t b -> p t c b")).then_inc(y_rows_ready, 1)

            def pre_high(n, half, s, par):
                dve.wait_ge(rec_done[half], n + 1)
                v.scalar_tensor_tensor(out=pre_hi[:, HALVES[half]], in0=rec_ps[half][:, :, 0, 0:B], scalar=wh_down[:],
                                       in1=xw[:, par, HALVES[half], s * B:(s + 1) * B], op0=ALU.mult,
                                       op1=ALU.add).then_inc(pre_part[half], 1)

            def pre_cross(n, half):
                dve.wait_ge(pre_part[half], n + 1)
                v.scalar_tensor_tensor(out=pre[:, HALVES[half]], in0=rec_ps[half][:, :, 1, 0:B], scalar=wh_down_lo[:],
                                       in1=pre_hi[:, HALVES[half]], op0=ALU.mult,
                                       op1=ALU.add).then_inc(pre_ready[half], 1)

            def h_low(n, half, s):
                dve.wait_ge(h_ready[half], n + 1).then_inc(h_seen[half], 1)
                v.tensor_tensor_reduce(out=h_parts[:, HALVES[half], 1, :],
                                       in0=h_ps[:, HALVES[half], s % (2 * GROUP), :],
                                       in1=h_parts[:, HALVES[half], 0, :], scale=LO, scalar=0.0, op0=ALU.subtract,
                                       op1=ALU.max, accum_out=lo_max[:, half:half + 1]).then_inc(h_lo_ready[half], 1)

            def block_body(i, rec, prod, turn, par):
                if i_is(i, -1):
                    setup_layer0()
                for s in range(STEPS):
                    n = i * STEPS + s
                    if rec:
                        if s == 0:
                            dve.wait_ge(xw_ready, i * FC + FC)
                        pre_high(n, 0, s, par)
                        pre_high(n, 1, s, par)
                        pre_cross(n, 0)
                        pre_cross(n, 1)
                        if s in TURN_OUT_AT and not (i_is(i, 0) and s == 1):
                            grp = TURN_OUT_AT[s]
                            turn_out(i if s > 1 else i - 1, grp)
                    if prod and s in SCALE_OUT_AT:
                        scale_out(i + 1, SCALE_OUT_AT[s])
                    if turn and s in TURN_IN_AT:
                        turn_in(i + 2, TURN_IN_AT[s], par)
                    if i_is(i, -1) and s == max(SCALE_OUT_AT):
                        setup_recurrence()
                    if rec:
                        for half in range(2):
                            h_low(n, half, s)
                        if s % GROUP == GROUP - 1:
                            sum_out(s // GROUP, 0, par)
                        if s % GROUP == 0 and not i_is(n, 0):
                            sum_out((s // GROUP - 1) % NG, 1, par if s else 1 - par)
                if i_is(i, -1):
                    dve.wait_ge(xw_ready, FC)
                    dve.wait_ge(first_done, 1)
                    link(v.tensor_tensor(xw[:, 0, :, 0:B], setup_ps, xw[:, 0, :, 0:B], ALU.add))

            run_blocks(dve, block_body, True)
            sum_out(NG - 1, 1, (NBLK - 1) % 2)
            turn_out(NBLK - 1, NG - 1)

        @block.scalar
        def _(act):
            a = nc.scalar

            def xs_high(n, grp):
                act.wait_ge(xs_ready, n * NG + grp + 1)
                if grp == 0 and not i_is(n, 0):
                    act.wait_ge(z_done, n * FC)
                a.activation(xs_hi[:, :, grp * GCOLS:(grp + 1) * GCOLS], xs[:, grp], ACT.Copy).then_inc(xs_hi_ready, 1)

            def x1_high(n, m, par):
                act.wait_ge(x1_ready, n * FC + m + 1)
                if m == 0 and not i_is(n, 0):
                    act.wait_ge(xw_done, n * FC)
                a.activation(x1_hi[:, m, :], x1[:, par, m, :], ACT.Copy).then_inc(x1_hi_ready, 1)

            def xw_out(n, m, par):
                act.wait_ge(xw_done, n * FC + m + 1)
                a.activation(xw[:, par, m, :], mm_ps[m][:], ACT.Identity, bias=bias_t[:, m:m + 1]).then_inc(xw_ready, 1)

            def step(n, s):
                for half in range(2):
                    act.wait_ge(pre_ready[half], n + 1)
                    a.activation(h_parts[:, HALVES[half], 0, :], pre[:, HALVES[half]], ACT.Tanh).then_inc(h_hi_ready[half], 1)
                for half in range(2):
                    a.activation(h_ps[:, HALVES[half], s % (2 * GROUP), :], pre[:, HALVES[half]],
                                 ACT.Tanh).then_inc(h_ready[half], 1)

            def block_body(i, rec, prod, turn, par):
                if i_is(i, -1):
                    act.wait_ge(wx_in, NQ * 16)
                    for k in range(FC):
                        a.activation(part_chunks(wx_hi, k), raw_chunks(wx_raw, k), ACT.Copy).then_inc(wx_hi_ready, 1)
                    act.wait_ge(wh_in, NQ * 16)
                    for k in range(FC):
                        a.activation(part_chunks(wh_cols, k), raw_chunks(wh_raw, k), ACT.Copy).then_inc(wh_cols_ready, 1)
                for s in range(STEPS):
                    if rec:
                        step(i * STEPS + s, s)
                    if prod:
                        if s in X1_HIGH_AT:
                            x1_high(i + 1, X1_HIGH_AT[s], 1 - par)
                    if turn and s in XS_HIGH_AT:
                        xs_high(i + 2, XS_HIGH_AT[s])
                    if prod and s in XW_OUT_AT:
                        xw_out(i + 1, XW_OUT_AT[s], 1 - par)
                if i_is(i, -2):
                    act.wait_ge(d_var_ready, 1)
                    a.activation(d_root[:], d_var[:], ACT.Sqrt).then_inc(d_root_ready, 1)
                    act.wait_ge(bias_in, NQ * 16)
                    a.activation(table_warm[:], bias_t[:], ACT.Tanh)

            with nc.allow_non_contiguous_dma(reason="512 values of the bias, once"):
                bias_quarters = bias.rearrange("(q c f) -> q f c", q=NQ, c=FC)
                for q in range(NQ):
                    act.dma_start(bias_t[q * SQ:(q + 1) * SQ], bias_quarters[q]).then_inc(bias_in, 16)
            act.wait_ge(w0_in, NQ * 16)
            for k in range(FC):
                a.activation(part_chunks(w0_hi, k), raw_chunks(w0_raw, k), ACT.Copy).then_inc(w0_hi_ready, 1)
            run_blocks(act, block_body, True)

        @block.tensor
        def _(pe):
            mm = nc.tensor.matmul

            def cols(m):
                return slice(m * P, (m + 1) * P)

            def setup_layer0():
                pe.wait_ge(ys_sq_ready, 1)
                pe.wait_ge(w_sq_ready, FC)
                for m in range(FC):
                    for k in range(FC):
                        last = mm(setup_ps[:, m, :], w_sq[:, k, cols(m)], ys_sq[:, k, :],
                                  start=(k == 0), stop=(k == FC - 1))
                last.then_inc(var_done, 1)

            def setup_recurrence():
                pe.wait_ge(wh_cols_ready, FC)
                pe.wait_ge(d_var_ready, 1)
                for m in range(FC):
                    for k in range(FC):
                        last = mm(setup_ps[:, m, :], wh_cols[:, k, cols(m)], cond_t[:, k, :],
                                  start=(k == 0), stop=(k == FC - 1))
                last.then_inc(first_done, 1)

            def product(m, half, w_h, w_l, v_h, v_l, before_chunk=None):
                for k in range(FC)[HALVES[half]]:
                    if before_chunk is not None:
                        before_chunk(k)
                    mm(mm_ps[m][:], w_l[:, k, cols(m)], v_h[:, k, :], start=(k == 0), stop=False)
                    mm(mm_ps[m][:], w_h[:, k, cols(m)], v_h[:, k, :], start=False, stop=False)
                    last = mm(mm_ps[m][:], w_h[:, k, cols(m)], v_l[:, k, :], start=False, stop=(k == FC - 1))
                return last

            def layer0_unit(n, u):
                m, half = LAYER0_UNITS[u]
                if u == 0:
                    pe.wait_ge(xs_hi_ready, n * NG + NG)
                    pe.wait_ge(xs_lo_ready, n * NG + NG)
                if half == 0 and not i_is(n, 0):
                    pe.wait_ge(xw_ready, (n - 1) * FC + m + 1)
                last = product(m, half, w0_hi, w0_lo, xs_hi, xs_lo)
                if half:
                    last.then_inc(z_done, 1)

            def layer1_unit(n, u):
                m, half = LAYER1_UNITS[u]

                def x1_chunk(k):
                    pe.wait_ge(x1_hi_ready, n * FC + k + 1)
                    pe.wait_ge(x1_lo_ready, n * FC + k + 1)

                if half == 0:
                    pe.wait_ge(zd_ready, n * FC + m + 1)
                last = product(m, half, wx_hi, wx_lo, x1_hi, x1_lo, x1_chunk if m == 0 else None)
                if half:
                    last.then_inc(xw_done, 1)

            def step(i, s):
                n = i * STEPS + s

                def cross(half, ks):
                    for m in range(FC)[HALVES[half]]:
                        for k in ks:
                            mm(rec_ps[half][:, m % 2, 1, 0:B], wh_lo[:, k, cols(m)], h_parts[:, k, 0, :],
                               start=(m % 2 == 0 and k == 0), stop=False, skip_group_check=True)

                pe.wait_ge(h_hi_ready[0], n + 1)
                cross(0, (0, 1))
                if not i_is(n, 0):
                    pe.wait_ge(pre_ready[1], n)
                cross(1, (0, 1))
                if not i_is(n, 0):
                    pe.wait_ge(h_hi_ready[1], n)
                cross(0, (2, 3))
                cross(1, (2, 3))
                for k_half in range(2):
                    if not i_is(n, 0):
                        pe.wait_ge(h_lo_ready[k_half], n)
                    for half in range(2):
                        for m in range(FC)[HALVES[half]]:
                            for k in range(FC)[HALVES[k_half]]:
                                last = mm(rec_ps[half][:, m % 2, :, 0:B], wh_hi[:, k, cols(m)], h_parts[:, k, :, :],
                                          start=False, stop=(m % 2 == 1 and k == FC - 1), skip_group_check=True)
                        if k_half:
                            last.then_inc(rec_done[half], 1)

            def block_body(i, rec, prod, turn, par):
                if i_is(i, -1):
                    setup_layer0()
                    pe.wait_ge(w0_ready, FC)
                if i_is(i, 0):
                    pe.wait_ge(wh_ready, 1)
                for s in range(STEPS):
                    if rec:
                        step(i, s)
                    if i_is(i, -1) and s == STEPS // 2:
                        setup_recurrence()
                        pe.wait_ge(wx_ready, FC)
                    if prod and s < STEPS // 2:
                        layer0_unit(i + 1, s)
                    if prod and s >= STEPS // 2:
                        layer1_unit(i + 1, s - STEPS // 2)

            run_blocks(pe, block_body, False)


_INS = ["x", "cond_1024", "L0_cond_weight", "L1_cond_Wx", "L1_cond_Wh", "L1_cond_b"]


def kernel(**inputs):
    import numpy as np
    import concourse.bacc as bacc
    from concourse.bass_utils import run_bass_kernel_spmd

    nc = bacc.Bacc("TRN2", target_bir_lowering=False, num_devices=1)
    arrays, args = {}, []
    for name in _INS:
        a = np.ascontiguousarray(inputs[name])
        arrays[f"in_{name}_dram"] = a
        args.append(nc.dram_tensor(f"in_{name}_dram", a.shape, mybir.dt.from_np(a.dtype), kind="ExternalInput").ap())
    shape = inputs["x"].shape
    out = nc.dram_tensor("out_dram", shape, FP32, kind="ExternalOutput").ap()
    cond_resid_kernel(nc, *args, out)
    r = run_bass_kernel_spmd(nc, [arrays], core_ids=[0])
    return r.results[0]["out_dram"]
```

```python
from contextlib import ExitStack

import concourse.bass as bass
from concourse import mybir

FP32 = mybir.dt.float32
FP32R = mybir.dt.float32r
FP16 = mybir.dt.float16
I32 = mybir.dt.int32
ALU = mybir.AluOpType
ACT = mybir.ActivationFunctionType
AX = mybir.AxisListType

P = 128
SQ = 32
EPS = 1e-8
LO = 1024.0
STEPS = 16
GROUP = 4
NG = STEPS // GROUP
STAGES = 3


def i_is(value, number):
    return isinstance(value, int) and value == number


def cond_resid_kernel(nc, x, cond, w0, wx, wh, bias, out):
    B, SEQ, F = x.shape
    FC = F // P
    NQ = P // SQ
    COLS = STEPS * B
    GCOLS = GROUP * B
    NBLK = SEQ // STEPS
    assert B == SQ and COLS == 512 and F == NQ * P and FC == NQ
    YSCALE = float(1.0 / F ** 0.5)
    HALVES = (slice(0, FC // 2), slice(FC // 2, FC))

    PAIR = 2 * GROUP
    x_blocks = x.rearrange("b (i t) (q n) -> i q b t n", t=STEPS, q=NQ)
    out_pairs = out.rearrange("b (j t) (q n) -> j q b t n", t=PAIR, q=NQ)

    with ExitStack() as ctx:
        def sb(name, shape, dt=FP32):
            return ctx.enter_context(nc.sbuf_tensor(name, shape, dt))

        def pb(name, shape=(P, 512)):
            return ctx.enter_context(nc.psum_tensor(name, list(shape), FP32))

        def sem(name):
            return ctx.enter_context(nc.semaphore(name))

        w0_raw, wx_raw, wh_raw = (sb(n, [P, FC, F]) for n in ("w0_raw", "wx_raw", "wh_raw"))
        w0_hi, w0_lo, wx_hi, wx_lo = (sb(n, [P, FC, F], FP32R) for n in ("w0_hi", "w0_lo", "wx_hi", "wx_lo"))
        wh_hi, wh_lo = (sb(n, [P, FC, F], FP16) for n in ("wh_hi", "wh_lo"))

        def raw_chunks(w, k):
            return w[:, k, :].rearrange("p (q m f) -> p m q f", q=NQ, m=FC)

        def part_chunks(w, k):
            return w[:, k, :].rearrange("p (m q f) -> p m q f", q=NQ, m=FC)

        bias_t = sb("bias_t", [P, FC])
        cond_rows = sb("cond_rows", [P, P])
        cond_t = sb("cond_t", [P, FC, B])
        ys_sq = sb("ys_sq", [P, FC, B])
        ys_t = sb("ys_t", [P, FC, B])
        d_var, d_root, d_inv, d_t = (sb(n, [P, FC, B]) for n in ("d_var", "d_root", "d_inv", "d_t"))
        wh_max, wh_max_all = sb("wh_max", [P, 1]), sb("wh_max_all", [P, 1])
        exps = sb("exps", [P, 3], I32)
        wh_up, wh_down, wh_down_lo = (sb(n, [P, 1]) for n in ("wh_up", "wh_down", "wh_down_lo"))
        table_warm = sb("table_warm", [P, FC])

        def over_time(columns, steps):
            return columns.unsqueeze(len(columns.shape) - 1).broadcast_to([*columns.shape[:-1], steps, B])

        ys_over_time = over_time(ys_t[:], GROUP)

        x_rows = sb("x_rows", [P, STEPS, FC, SQ])
        x_t = sb("x_t", [P, 2, FC, STEPS, B])
        xs = sb("xs", [P, NG, FC, GROUP, B])
        xs_hi, xs_lo = (sb(n, [P, FC, COLS], FP32R) for n in ("xs_hi", "xs_lo"))
        zd = sb("zd", [P, 2, COLS])
        x1 = sb("x1", [P, 2, FC, COLS])
        x1_hi, x1_lo = (sb(n, [P, FC, COLS], FP32R) for n in ("x1_hi", "x1_lo"))
        xw = sb("xw", [P, 2, FC, COLS])
        pre_hi, pre = sb("pre_hi", [P, FC, B]), sb("pre", [P, FC, B])
        h_parts = sb("h_parts", [P, FC, 2, B], FP16)
        lo_max = sb("lo_max", [P, 2])
        y_t = sb("y_t", [P, 2, FC, GROUP, B])
        y_rows = sb("y_rows", [P, STEPS, FC, SQ])
        def xs_columns(grp):
            return xs[:, grp].rearrange("p c t b -> p c (t b)")

        w_sq, wh_cols = x1[:, 0], x1[:, 1]

        rec_ps = [pb(f"rec_ps{i}", (P, FC // 2, 2, P)) for i in range(2)]
        h_ps = pb("h_ps", (P, FC, 2 * GROUP, B))
        mm_ps = [pb(f"mm_ps{i}") for i in range(4)]
        setup_ps = h_ps[:, :, 0, :]

        w0_in, wx_in, wh_in, cond_in, bias_in = (sem(n) for n in ("w0_in", "wx_in", "wh_in", "cond_in", "bias_in"))
        x_loaded = sem("x_loaded")
        stored = [sem(f"stored{k}") for k in range(2)]
        cond_ready, ys_sq_ready, w_sq_ready, d_var_ready, d_root_ready = (
            sem(n) for n in ("cond_ready", "ys_sq_ready", "w_sq_ready", "d_var_ready", "d_root_ready"))
        var_done, first_done, max_ready, max_all_ready = (
            sem(n) for n in ("var_done", "first_done", "max_ready", "max_all_ready"))
        w0_hi_ready, w0_ready, wx_hi_ready, wx_ready, wh_cols_ready, wh_ready, dve_done = (
            sem(n) for n in ("w0_hi_ready", "w0_ready", "wx_hi_ready", "wx_ready", "wh_cols_ready", "wh_ready", "dve_done"))
        x_turned, xs_ready, xs_hi_ready, xs_lo_ready = (
            sem(n) for n in ("x_turned", "xs_ready", "xs_hi_ready", "xs_lo_ready"))
        z_done, zd_ready, x1_ready, x1_hi_ready, x1_lo_ready = (
            sem(n) for n in ("z_done", "zd_ready", "x1_ready", "x1_hi_ready", "x1_lo_ready"))
        xw_done, xw_ready = sem("xw_done"), sem("xw_ready")
        rec_done, pre_part, pre_ready, h_hi_ready, h_ready, h_seen, h_lo_ready = (
            [sem(f"{n}{i}") for i in range(2)] for n in ("rec_done", "pre_part", "pre_ready", "h_hi_ready", "h_ready",
                                                         "h_seen", "h_lo_ready"))
        y_ready, y_rows_ready = sem("y_ready"), sem("y_rows_ready")

        FIRST, LOOP_FROM, LOOP_TO = -2, 2, NBLK - 2
        assert LOOP_FROM % 2 == 0 and (LOOP_TO - LOOP_FROM) % 2 == 0

        def run_blocks(engine, block_body, pairs):
            for i in range(FIRST, LOOP_FROM):
                block_body(i, i >= 0, i >= -1, True, i % 2)
            if pairs:
                with nc.Fori(0, (LOOP_TO - LOOP_FROM) // 2, engines=[engine.engine], hint_back_edge=True) as j:
                    for parity in range(2):
                        block_body(j * 2 + (LOOP_FROM + parity), True, True, True, parity)
            else:
                with nc.Fori(LOOP_FROM, LOOP_TO, engines=[engine.engine], hint_back_edge=True) as i:
                    block_body(i, True, True, True, None)
            for i in range(LOOP_TO, NBLK):
                block_body(i, True, i + 1 < NBLK, i + 2 < NBLK, i % 2)

        TURN_LAST_AT = 5
        TURN_OUT_AT = {TURN_LAST_AT: 3, 7: 0, 10: 1, 13: 2}
        SCALE_OUT_AT = {2: 0, 4: 1, 6: 2, 8: 3}
        TURN_IN_AT = {3: 0, 9: 1, 11: 2, 12: 3}
        X1_HIGH_AT = {3: 0, 5: 1, 7: 2, 9: 3}
        XS_HIGH_AT = {8: 0, 11: 1, 13: 2, 14: 3}
        XW_OUT_AT = {12: 0, 13: 1, 14: 2, 15: 3}
        LAYER0_UNITS = [(m, half) for m in range(FC) for half in range(2)]
        LAYER1_UNITS = [(0, 0), (1, 0), (2, 0), (0, 1), (1, 1), (3, 0), (2, 1), (3, 1)]

        block = ctx.enter_context(nc.Block())

        @block.sync
        def _(sp):
            def quarter(q):
                return slice(q * SQ, (q + 1) * SQ)

            def load_weight(w_raw, w, loaded):
                rows = w.rearrange("(q c f) n -> q f c n", q=NQ, c=FC)
                for q in range(NQ):
                    sp.dma_start(w_raw[quarter(q)], rows[q]).then_inc(loaded, 16)

            def load(n):
                if not i_is(n, 0):
                    sp.wait_ge(x_turned, n * NG)
                for q in range(NQ):
                    sp.dma_start(x_rows[quarter(q)].rearrange("p t c f -> p t (c f)"), x_blocks[n, q]).then_inc(x_loaded, 16)

            def store(i, pair):
                sp.wait_ge(y_rows_ready, i * NG + 2 * pair + 2)
                for q in range(NQ):
                    sp.dma_start(out_pairs[i * 2 + pair, q],
                                 y_rows[quarter(q), pair * PAIR:(pair + 1) * PAIR].rearrange("p t c f -> p t (c f)")
                                 ).then_inc(stored[pair], 16)

            cond_quarters = cond.rearrange("b (q n) -> q b n", q=NQ)
            for q in range(NQ):
                sp.dma_start(cond_rows[quarter(q)], cond_quarters[q]).then_inc(cond_in, 16)
            load_weight(w0_raw, w0, w0_in)
            load(0)
            load_weight(wx_raw, wx, wx_in)
            load_weight(wh_raw, wh, wh_in)

            def block_body(i, load_next):
                if not i_is(i, 0):
                    store(i - 1, 1)
                if load_next:
                    load(i + 3)
                store(i, 0)

            load(1)
            load(2)
            for i in range(LOOP_FROM):
                block_body(i, True)
            with sp.Fori(LOOP_FROM, NBLK - STAGES) as i:
                block_body(i, True)
            for i in range(NBLK - STAGES, NBLK):
                block_body(i, False)
            store(NBLK - 1, 1)
            for pair in range(2):
                sp.wait_ge(stored[pair], NBLK * NQ * 16)

        @block.gpsimd
        def _(pool):
            g = nc.gpsimd

            def scale_in(n, grp, par):
                pool.wait_ge(x_turned, n * NG + grp + 1)
                g.tensor_tensor(xs[:, grp], x_t[:, par, :, grp * GROUP:(grp + 1) * GROUP, :], ys_over_time,
                                ALU.mult).then_inc(xs_ready, 1)

            def xs_low(n, grp):
                pool.wait_ge(xs_hi_ready, n * NG + grp + 1)
                cols = slice(grp * GCOLS, (grp + 1) * GCOLS)
                g.tensor_tensor(xs_lo[:, :, cols], xs_columns(grp), xs_hi[:, :, cols].bitcast(FP32),
                                ALU.subtract).then_inc(xs_lo_ready, 1)

            def x1_sum(n, m, par):
                pool.wait_ge(zd_ready, n * FC + m + 1)
                g.tensor_tensor(x1[:, par, m, :], zd[:, m % 2, :], x_t[:, par, m].rearrange("p t b -> p (t b)"),
                                ALU.add).then_inc(x1_ready, 1)

            def x1_low(n, m, par):
                pool.wait_ge(x1_hi_ready, n * FC + m + 1)
                g.tensor_tensor(x1_lo[:, m, :], x1[:, par, m, :], x1_hi[:, m, :].bitcast(FP32),
                                ALU.subtract).then_inc(x1_lo_ready, 1)

            def block_body(i, rec, prod, turn, par):
                if i_is(i, -2):
                    pool.wait_ge(w0_in, NQ * 16)
                    g.tensor_tensor(part_chunks(w_sq, 0), raw_chunks(w0_raw, 0), raw_chunks(w0_raw, 0),
                                    ALU.mult).then_inc(w_sq_ready, 1)
                    for k in (2, 3):
                        pool.wait_ge(w0_hi_ready, k + 1)
                        g.tensor_tensor(part_chunks(w0_lo, k), raw_chunks(w0_raw, k),
                                        part_chunks(w0_hi, k).bitcast(FP32), ALU.subtract).then_inc(w0_ready, 1)
                    for grp in range(NG - 1):
                        xs_low(0, grp)
                    for k in (0, 1):
                        pool.wait_ge(wx_hi_ready, k + 1)
                        g.tensor_tensor(part_chunks(wx_lo, k), raw_chunks(wx_raw, k),
                                        part_chunks(wx_hi, k).bitcast(FP32), ALU.subtract).then_inc(wx_ready, 1)
                    pool.wait_ge(max_ready, 1)
                    g.partition_all_reduce(wh_max_all[:], wh_max[:], P, bass.bass_isa.ReduceOp.max).then_inc(max_all_ready, 1)
                    return
                if i_is(i, -1):
                    for m in range(FC):
                        x1_sum(0, m, 1 - par)
                        scale_in(1, m, par)
                    for grp in range(NG):
                        xs_low(1, grp)
                    return
                if prod:
                    x1_sum(i + 1, 0, 1 - par)
                if turn:
                    scale_in(i + 2, 0, par)
                if prod:
                    x1_low(i + 1, 0, 1 - par)
                    for m in (1, 2):
                        x1_sum(i + 1, m, 1 - par)
                        x1_low(i + 1, m, 1 - par)
                    x1_sum(i + 1, 3, 1 - par)
                    x1_low(i + 1, 3, 1 - par)
                if turn:
                    scale_in(i + 2, 1, par)
                    xs_low(i + 2, 0)
                    scale_in(i + 2, 2, par)
                    xs_low(i + 2, 1)
                    scale_in(i + 2, 3, par)
                    xs_low(i + 2, 2)
                    xs_low(i + 2, 3)

            pool.wait_ge(ys_sq_ready, 1)
            run_blocks(pool, block_body, True)

        @block.vector
        def _(dve):
            v = nc.vector
            done = [0]

            def link(ins):
                done[0] += 1
                ins.then_inc(dve_done, 1)
                dve.wait_ge(dve_done, done[0])

            v.memset(h_parts[:], 0.0).then_inc(h_hi_ready[0], 1)
            dve.wait_ge(cond_in, NQ * 16)
            v.transpose(cond_t[:], cond_rows[:].rearrange("p (c f) -> p c f", c=FC)).then_inc(cond_ready, 1)
            dve.wait_ge(cond_ready, 1)
            link(v.tensor_scalar(ys_t[:], cond_t[:], YSCALE, None, ALU.mult))
            v.tensor_tensor(ys_sq[:], ys_t[:], ys_t[:], ALU.mult).then_inc(ys_sq_ready, 1)

            def setup_first_products():
                dve.wait_ge(w0_in, NQ * 16)
                for k in range(1, FC):
                    v.tensor_tensor(part_chunks(w_sq, k), raw_chunks(w0_raw, k), raw_chunks(w0_raw, k),
                                    ALU.mult).then_inc(w_sq_ready, 1)
                for k in (0, 1):
                    dve.wait_ge(w0_hi_ready, k + 1)
                    v.tensor_tensor(part_chunks(w0_lo, k), raw_chunks(w0_raw, k),
                                    part_chunks(w0_hi, k).bitcast(FP32), ALU.subtract).then_inc(w0_ready, 1)
                for grp in range(NG):
                    turn_in(0, grp, 0)
                    dve.wait_ge(x_turned, grp + 1)
                    v.tensor_tensor(xs[:, grp], x_t[:, 0, :, grp * GROUP:(grp + 1) * GROUP, :], ys_over_time,
                                    ALU.mult).then_inc(xs_ready, 1)

            def setup_wh_max():
                dve.wait_ge(wh_in, NQ * 16)
                v.tensor_reduce(wh_max[:], wh_raw[:].rearrange("p c n -> p (c n)"), AX.X, ALU.max,
                                apply_absolute_value=True).then_inc(max_ready, 1)

            wh_scaled = w0_raw

            def setup_wh():
                dve.wait_ge(max_all_ready, 1)
                link(v.tensor_single_scalar(exps[:, 0:1], wh_max_all[:].bitcast(I32), 23, op=ALU.logical_shift_right))
                link(v.tensor_scalar(exps[:, 0:1], exps[:, 0:1], 32.0, None, ALU.max))
                v.tensor_scalar(exps[:, 1:2], exps[:, 0:1], -1.0, 268.0, ALU.mult, ALU.add)
                link(v.tensor_scalar(exps[:, 2:3], exps[:, 0:1], -14.0, None, ALU.add))
                v.tensor_single_scalar(wh_up[:].bitcast(I32), exps[:, 1:2], 23, op=ALU.logical_shift_left)
                link(v.tensor_single_scalar(wh_down[:].bitcast(I32), exps[:, 2:3], 23, op=ALU.logical_shift_left))
                v.tensor_scalar(wh_down_lo[:], wh_down[:], 1.0 / LO, None, ALU.mult)
                dve.wait_ge(wh_cols_ready, FC)
                dve.wait_ge(w_sq_ready, FC)
                dve.wait_ge(w0_ready, FC)
                link(v.tensor_scalar(wh_scaled[:], wh_cols, wh_up[:], None, ALU.mult))
                link(v.tensor_copy(wh_hi[:], wh_scaled[:]))
                link(v.tensor_tensor(wh_scaled[:], wh_scaled[:], wh_hi[:], ALU.subtract))
                v.tensor_scalar(wh_lo[:], wh_scaled[:], LO, None, ALU.mult).then_inc(wh_ready, 1)

            def setup_d():
                dve.wait_ge(var_done, 1)
                v.tensor_scalar(d_var[:], setup_ps, EPS, None, ALU.add).then_inc(d_var_ready, 1)
                dve.wait_ge(xs_hi_ready, NG)
                v.tensor_tensor(xs_lo[:, :, (NG - 1) * GCOLS:], xs_columns(NG - 1),
                                xs_hi[:, :, (NG - 1) * GCOLS:].bitcast(FP32), ALU.subtract).then_inc(xs_lo_ready, 1)
                dve.wait_ge(d_root_ready, 1)
                link(v.reciprocal(d_inv[:], d_root[:]))
                link(v.tensor_tensor(d_var[:], d_var[:], d_inv[:], ALU.mult))
                link(v.tensor_tensor(d_var[:], d_var[:], d_inv[:], ALU.mult))
                link(v.tensor_scalar(d_var[:], d_var[:], -0.5, 1.5, ALU.mult, ALU.add))
                link(v.tensor_tensor(d_t[:], d_var[:], d_inv[:], ALU.mult))

            def first_block():
                def x1_low(m):
                    dve.wait_ge(x1_hi_ready, m + 1)
                    v.tensor_tensor(x1_lo[:, m, :], x1[:, 0, m, :], x1_hi[:, m, :].bitcast(FP32),
                                    ALU.subtract).then_inc(x1_lo_ready, 1)

                def wx_low(k):
                    dve.wait_ge(wx_hi_ready, k + 1)
                    v.tensor_tensor(part_chunks(wx_lo, k), raw_chunks(wx_raw, k),
                                    part_chunks(wx_hi, k).bitcast(FP32), ALU.subtract).then_inc(wx_ready, 1)

                for m in range(FC):
                    scale_out(0, m)
                    turn_in(1, m, 1)
                    if m:
                        x1_low(m - 1)
                    if m < 2:
                        wx_low(m + 2)
                x1_low(FC - 1)
                setup_wh()
                dve.wait_ge(xw_ready, FC)
                dve.wait_ge(first_done, FC)
                link(v.tensor_tensor(xw[:, 0, :, 0:B], setup_ps, xw[:, 0, :, 0:B], ALU.add))

            def turn_in(n, grp, par):
                if grp == 0:
                    dve.wait_ge(x_loaded, (n + 1) * (NQ * 16))
                v.transpose(x_t[:, par, :, grp * GROUP:(grp + 1) * GROUP, :].rearrange("p c t b -> p t c b"),
                            x_rows[:, grp * GROUP:(grp + 1) * GROUP]).then_inc(x_turned, 1)

            def scale_out(n, m):
                dve.wait_ge(z_done, n * FC + m + 1)
                if not (i_is(n, 0) and m < 2):
                    dve.wait_ge(x1_ready, n * FC + m - 1)
                v.tensor_tensor(zd[:, m % 2, :].rearrange("p (t b) -> p t b", t=STEPS),
                                mm_ps[m][:].rearrange("p (t b) -> p t b", t=STEPS), over_time(d_t[:, m, :], STEPS),
                                ALU.mult).then_inc(zd_ready, 1)

            def sum_out(grp, half, par):
                c, at = HALVES[half], grp % 2 * GROUP
                v.tensor_tensor(y_t[:, grp % 2, c], h_ps[:, c, at:at + GROUP, :],
                                x1[:, par, c, grp * GCOLS:(grp + 1) * GCOLS].rearrange("p c (t b) -> p c t b", t=GROUP),
                                ALU.add).then_inc(y_ready, 1)

            def turn_out(i, grp):
                dve.wait_ge(y_ready, (i * NG + grp + 1) * 2)
                if grp % 2 == 0 and not i_is(i, 0):
                    dve.wait_ge(stored[grp // 2], i * (NQ * 16))
                v.transpose(y_rows[:, grp * GROUP:(grp + 1) * GROUP], y_t[:, grp % 2].rearrange("p c t b -> p t c b")).then_inc(y_rows_ready, 1)

            def pre_high(n, half, s, par):
                dve.wait_ge(rec_done[half], n + 1)
                v.scalar_tensor_tensor(out=pre_hi[:, HALVES[half]], in0=rec_ps[half][:, :, 0, 0:B], scalar=wh_down[:],
                                       in1=xw[:, par, HALVES[half], s * B:(s + 1) * B], op0=ALU.mult,
                                       op1=ALU.add).then_inc(pre_part[half], 1)

            def pre_cross(n, half):
                dve.wait_ge(pre_part[half], n + 1)
                v.scalar_tensor_tensor(out=pre[:, HALVES[half]], in0=rec_ps[half][:, :, 1, 0:B], scalar=wh_down_lo[:],
                                       in1=pre_hi[:, HALVES[half]], op0=ALU.mult,
                                       op1=ALU.add).then_inc(pre_ready[half], 1)

            def h_low(n, half, s):
                dve.wait_ge(h_ready[half], n + 1).then_inc(h_seen[half], 1)
                v.tensor_tensor_reduce(out=h_parts[:, HALVES[half], 1, :],
                                       in0=h_ps[:, HALVES[half], s % (2 * GROUP), :],
                                       in1=h_parts[:, HALVES[half], 0, :], scale=LO, scalar=0.0, op0=ALU.subtract,
                                       op1=ALU.max, accum_out=lo_max[:, half:half + 1]).then_inc(h_lo_ready[half], 1)

            def block_body(i, rec, prod, turn, par):
                if i_is(i, -2):
                    setup_first_products()
                    return
                if i_is(i, -1):
                    setup_d()
                    setup_wh_max()
                    first_block()
                    return
                for s in range(STEPS):
                    n = i * STEPS + s
                    if rec:
                        if s == 0:
                            dve.wait_ge(xw_ready, i * FC + FC)
                        pre_high(n, 0, s, par)
                        pre_high(n, 1, s, par)
                        pre_cross(n, 0)
                        pre_cross(n, 1)
                        if s in TURN_OUT_AT and not (i_is(i, 0) and s == TURN_LAST_AT):
                            grp = TURN_OUT_AT[s]
                            turn_out(i - 1 if s == TURN_LAST_AT else i, grp)
                    if prod and s in SCALE_OUT_AT:
                        scale_out(i + 1, SCALE_OUT_AT[s])
                    if turn and s in TURN_IN_AT:
                        turn_in(i + 2, TURN_IN_AT[s], par)
                    if rec:
                        for half in range(2):
                            h_low(n, half, s)
                        if s % GROUP == GROUP - 1 and s != STEPS - 1:
                            sum_out(s // GROUP, 0, par)
                        if s % GROUP == 0 and s:
                            sum_out(s // GROUP - 1, 1, par)
                        if s < 2 and not i_is(i, 0):
                            sum_out(NG - 1, s, 1 - par)

            run_blocks(dve, block_body, True)
            for half in range(2):
                sum_out(NG - 1, half, (NBLK - 1) % 2)
            turn_out(NBLK - 1, NG - 1)

        @block.scalar
        def _(act):
            a = nc.scalar

            def xs_high(n, grp):
                act.wait_ge(xs_ready, n * NG + grp + 1)
                if grp == 0 and not i_is(n, 0):
                    act.wait_ge(z_done, n * FC)
                a.activation(xs_hi[:, :, grp * GCOLS:(grp + 1) * GCOLS], xs_columns(grp), ACT.Copy).then_inc(xs_hi_ready, 1)

            def x1_high(n, m, par):
                act.wait_ge(x1_ready, n * FC + m + 1)
                if m == 0 and not i_is(n, 0):
                    act.wait_ge(xw_done, n * FC)
                a.activation(x1_hi[:, m, :], x1[:, par, m, :], ACT.Copy).then_inc(x1_hi_ready, 1)

            def xw_out(n, m, par):
                act.wait_ge(xw_done, n * FC + m + 1)
                a.activation(xw[:, par, m, :], mm_ps[m][:], ACT.Identity, bias=bias_t[:, m:m + 1]).then_inc(xw_ready, 1)

            def step(n, s):
                for half in range(2):
                    act.wait_ge(pre_ready[half], n + 1)
                    a.activation(h_parts[:, HALVES[half], 0, :], pre[:, HALVES[half]], ACT.Tanh).then_inc(h_hi_ready[half], 1)
                    a.activation(h_ps[:, HALVES[half], s % (2 * GROUP), :], pre[:, HALVES[half]],
                                 ACT.Tanh).then_inc(h_ready[half], 1)

            def block_body(i, rec, prod, turn, par):
                if i_is(i, -2):
                    act.wait_ge(ys_sq_ready, 1)
                    a.activation(table_warm[:], ys_sq[:, :, 0], ACT.Sqrt)
                    act.wait_ge(w0_in, NQ * 16)
                    for k in range(FC):
                        a.activation(part_chunks(w0_hi, k), raw_chunks(w0_raw, k), ACT.Copy).then_inc(w0_hi_ready, 1)
                    for grp in range(NG):
                        xs_high(0, grp)
                    return
                if i_is(i, -1):
                    act.wait_ge(d_var_ready, 1)
                    a.activation(d_root[:], d_var[:], ACT.Sqrt).then_inc(d_root_ready, 1)
                    act.wait_ge(wx_in, NQ * 16)
                    for k in range(FC):
                        a.activation(part_chunks(wx_hi, k), raw_chunks(wx_raw, k), ACT.Copy).then_inc(wx_hi_ready, 1)
                    act.wait_ge(wh_in, NQ * 16)
                    for k in range(FC):
                        a.activation(part_chunks(wh_cols, k), raw_chunks(wh_raw, k), ACT.Copy).then_inc(wh_cols_ready, 1)
                    act.wait_ge(bias_in, NQ * 16)
                    a.activation(table_warm[:], bias_t[:], ACT.Tanh)
                    for m in range(FC):
                        x1_high(0, m, 0)
                    for grp in range(NG):
                        xs_high(1, grp)
                    for m in range(FC):
                        xw_out(0, m, 0)
                    return
                for s in range(STEPS):
                    if rec:
                        step(i * STEPS + s, s)
                    if prod:
                        if s in X1_HIGH_AT:
                            x1_high(i + 1, X1_HIGH_AT[s], 1 - par)
                    if turn and s in XS_HIGH_AT:
                        xs_high(i + 2, XS_HIGH_AT[s])
                    if prod and s in XW_OUT_AT:
                        xw_out(i + 1, XW_OUT_AT[s], 1 - par)

            with nc.allow_non_contiguous_dma(reason="512 values of the bias, once"):
                bias_quarters = bias.rearrange("(q c f) -> q f c", q=NQ, c=FC)
                for q in range(NQ):
                    act.dma_start(bias_t[q * SQ:(q + 1) * SQ], bias_quarters[q]).then_inc(bias_in, 16)
            run_blocks(act, block_body, True)

        @block.tensor
        def _(pe):
            mm = nc.tensor.matmul

            def cols(m):
                return slice(m * P, (m + 1) * P)

            def warm_up(turns):
                zeros = h_parts[:].rearrange("p c two b -> p (c two b)")
                pe.wait_ge(h_hi_ready[0], 1)
                with nc.Fori(0, turns, engines=[pe.engine]):
                    for bank in range(4):
                        for _ in range(2):
                            mm(mm_ps[bank][:, 0:2 * P], zeros[:, 0:P], zeros, start=True, stop=True)

            def keep_clock():
                for k in range(FC):
                    mm(mm_ps[k][:], w0_hi[:, k, 0:P], xs_hi[:, k, :], start=True, stop=True)

            def setup_variance():
                pe.wait_ge(ys_sq_ready, 1)
                pe.wait_ge(w_sq_ready, FC)
                for m in range(FC):
                    for k in range(FC):
                        last = mm(setup_ps[:, m, :], w_sq[:, k, cols(m)], ys_sq[:, k, :],
                                  start=(k == 0), stop=(k == FC - 1))
                last.then_inc(var_done, 1)

            def setup_recurrence(m):
                if m == 0:
                    pe.wait_ge(wh_cols_ready, FC)
                    pe.wait_ge(d_var_ready, 1)
                for k in range(FC):
                    last = mm(setup_ps[:, m, :], wh_cols[:, k, cols(m)], cond_t[:, k, :],
                              start=(k == 0), stop=(k == FC - 1))
                last.then_inc(first_done, 1)

            def product(m, half, w_h, w_l, v_h, v_l, before_chunk=None):
                for k in range(FC)[HALVES[half]]:
                    if before_chunk is not None:
                        before_chunk(k)
                    mm(mm_ps[m][:], w_l[:, k, cols(m)], v_h[:, k, :], start=(k == 0), stop=False)
                    mm(mm_ps[m][:], w_h[:, k, cols(m)], v_h[:, k, :], start=False, stop=False)
                    last = mm(mm_ps[m][:], w_h[:, k, cols(m)], v_l[:, k, :], start=False, stop=(k == FC - 1))
                return last

            def layer0_unit(n, u):
                m, half = LAYER0_UNITS[u]
                if u == 0:
                    pe.wait_ge(xs_hi_ready, n * NG + NG)
                    pe.wait_ge(xs_lo_ready, n * NG + NG)
                if half == 0 and not i_is(n, 0):
                    pe.wait_ge(xw_ready, (n - 1) * FC + m + 1)
                last = product(m, half, w0_hi, w0_lo, xs_hi, xs_lo)
                if half:
                    last.then_inc(z_done, 1)

            def layer1_unit(n, u):
                m, half = LAYER1_UNITS[u]

                def x1_chunk(k):
                    pe.wait_ge(x1_hi_ready, n * FC + k + 1)
                    pe.wait_ge(x1_lo_ready, n * FC + k + 1)

                if half == 0:
                    pe.wait_ge(zd_ready, n * FC + m + 1)
                last = product(m, half, wx_hi, wx_lo, x1_hi, x1_lo, x1_chunk if m == 0 else None)
                if half:
                    last.then_inc(xw_done, 1)

            def step(i, s):
                n = i * STEPS + s

                def cross(half, ks):
                    for m in range(FC)[HALVES[half]]:
                        for k in ks:
                            mm(rec_ps[half][:, m % 2, 1, 0:B], wh_lo[:, k, cols(m)], h_parts[:, k, 0, :],
                               start=(m % 2 == 0 and k == 0), stop=False, skip_group_check=True)

                pe.wait_ge(h_hi_ready[0], n + 1)
                cross(0, (0, 1))
                if not i_is(n, 0):
                    pe.wait_ge(pre_ready[1], n)
                cross(1, (0, 1))
                if not i_is(n, 0):
                    pe.wait_ge(h_hi_ready[1], n)
                cross(0, (2, 3))
                cross(1, (2, 3))
                for k_half in range(2):
                    if not i_is(n, 0):
                        pe.wait_ge(h_lo_ready[k_half], n)
                    for half in range(2):
                        for m in range(FC)[HALVES[half]]:
                            for k in range(FC)[HALVES[k_half]]:
                                last = mm(rec_ps[half][:, m % 2, :, 0:B], wh_hi[:, k, cols(m)], h_parts[:, k, :, :],
                                          start=False, stop=(m % 2 == 1 and k == FC - 1), skip_group_check=True)
                        if k_half:
                            last.then_inc(rec_done[half], 1)

            def block_body(i, rec, prod, turn, par):
                if i_is(i, -2):
                    warm_up(9)
                    setup_variance()
                    warm_up(5)
                    pe.wait_ge(w0_ready, FC)
                if i_is(i, 0):
                    pe.wait_ge(wh_ready, 1)
                if i_is(i, NBLK - 1):
                    pe.wait_ge(xw_ready, NBLK * FC)
                for s in range(STEPS):
                    if rec:
                        step(i, s)
                    if i_is(i, -1) and s == STEPS // 2:
                        pe.wait_ge(wx_ready, FC)
                    if prod and s < STEPS // 2:
                        layer0_unit(i + 1, s)
                    if i_is(i, NBLK - 1) and s < STEPS - 1:
                        keep_clock()
                    if prod and s >= STEPS // 2:
                        layer1_unit(i + 1, s - STEPS // 2)
                    if i_is(i, -1) and STEPS // 2 <= s < STEPS // 2 + FC:
                        setup_recurrence(s - STEPS // 2)

            run_blocks(pe, block_body, False)


_INS = ["x", "cond_1024", "L0_cond_weight", "L1_cond_Wx", "L1_cond_Wh", "L1_cond_b"]


def kernel(**inputs):
    import numpy as np
    import concourse.bacc as bacc
    from concourse.bass_utils import run_bass_kernel_spmd

    nc = bacc.Bacc("TRN2", target_bir_lowering=False, num_devices=1)
    arrays, args = {}, []
    for name in _INS:
        a = np.ascontiguousarray(inputs[name])
        arrays[f"in_{name}_dram"] = a
        args.append(nc.dram_tensor(f"in_{name}_dram", a.shape, mybir.dt.from_np(a.dtype), kind="ExternalInput").ap())
    shape = inputs["x"].shape
    out = nc.dram_tensor("out_dram", shape, FP32, kind="ExternalOutput").ap()
    cond_resid_kernel(nc, *args, out)
    r = run_bass_kernel_spmd(nc, [arrays], core_ids=[0])
    return r.results[0]["out_dram"]
```
